# Optimizing a Trainium2 kernel written in Bass

```python
import numpy as np
import jax
import jax.numpy as jnp

def _softmax(x, axis=-1):
    return jax.nn.softmax(x, axis=axis)

def _gelu(x):
    return jax.nn.gelu(x, approximate=True)

def _silu(x):
    return jax.nn.silu(x)

def _sigmoid(x):
    return jax.nn.sigmoid(x)

def _layernorm(x, axis=-1, eps=1e-05):
    m = jnp.mean(x, axis=axis, keepdims=True)
    v = jnp.var(x, axis=axis, keepdims=True)
    return (x - m) / jnp.sqrt(v + eps)

def _scatter_add(tgt, idx, src, axis=0):
    return tgt.at[idx].add(src)

def _segment_sum(src, seg, n):
    return jax.ops.segment_sum(src, seg, n)
kernel_name = 'mk_rec_standalone_d1_rec_r8_d322cd'

def setup_inputs(seed: int=0):
    np.random.seed(seed)
    _w = jnp.asarray

    def _rec_inputs():
        import jax
        import jax.numpy as jnp
        _rk = jax.random.key(seed)
        r_x = -0.00011082 + 0.999858 * jax.random.normal(jax.random.fold_in(_rk, 1), (2048, 40, 64), jnp.float32)
        return r_x
    r_x = _rec_inputs()

    def _L0_rec_setup():
        import jax, jax.numpy as jnp
        import numpy as np
        EMB = 64
        ATT = 32
        HEADS = 4
        OUT = ATT * HEADS
        key = jax.random.key(seed)
        ks = jax.random.split(key, 9)
        B, F = (2048, 40)
        x = jax.random.normal(ks[0], (B, F, EMB), dtype=jnp.float32)
        s = 0.05
        Wq = jax.random.normal(ks[1], (OUT, EMB), dtype=jnp.float32) * s
        bq = jax.random.normal(ks[2], (OUT,), dtype=jnp.float32) * s
        Wk = jax.random.normal(ks[3], (OUT, EMB), dtype=jnp.float32) * s
        bk = jax.random.normal(ks[4], (OUT,), dtype=jnp.float32) * s
        Wv = jax.random.normal(ks[5], (OUT, EMB), dtype=jnp.float32) * s
        bv = jax.random.normal(ks[6], (OUT,), dtype=jnp.float32) * s
        Wr = jax.random.normal(ks[7], (OUT, EMB), dtype=jnp.float32) * s
        br = jax.random.normal(ks[8], (OUT,), dtype=jnp.float32) * s
        return {'x': x, 'Wq': Wq, 'bq': bq, 'Wk': Wk, 'bk': bk, 'Wv': Wv, 'bv': bv, 'Wr': Wr, 'br': br}
    _L0_rec_all = _L0_rec_setup()
    _L0_rec_in = {k: v for k, v in _L0_rec_all.items() if k in ('Wq', 'bq', 'Wk', 'bk', 'Wv', 'bv', 'Wr', 'br')}
    del _L0_rec_all
    return {'r_x': r_x, 'L0_rec_Wq': _L0_rec_in['Wq'], 'L0_rec_bq': _L0_rec_in['bq'], 'L0_rec_Wk': _L0_rec_in['Wk'], 'L0_rec_bk': _L0_rec_in['bk'], 'L0_rec_Wv': _L0_rec_in['Wv'], 'L0_rec_bv': _L0_rec_in['bv'], 'L0_rec_Wr': _L0_rec_in['Wr'], 'L0_rec_br': _L0_rec_in['br']}

def reference(r_x, L0_rec_Wq, L0_rec_bq, L0_rec_Wk, L0_rec_bk, L0_rec_Wv, L0_rec_bv, L0_rec_Wr, L0_rec_br):
    import jax
    import jax.numpy as jnp

    def _L0_rec_ref(x, Wq, bq, Wk, bk, Wv, bv, Wr, br):
        import jax, jax.numpy as jnp
        import numpy as np
        EMB = 64
        ATT = 32
        HEADS = 4
        OUT = ATT * HEADS
        B, F, E = x.shape
        H, D = (HEADS, ATT)
        q = (jnp.einsum('bfe,oe->bfo', x, Wq) + bq).reshape(B, F, H, D)
        k = (jnp.einsum('bfe,oe->bfo', x, Wk) + bk).reshape(B, F, H, D)
        v = (jnp.einsum('bfe,oe->bfo', x, Wv) + bv).reshape(B, F, H, D)
        scale = 1.0 / jnp.sqrt(jnp.float32(E))
        att = jnp.einsum('bfhd,bghd->bhfg', q, k) * scale
        att = jax.nn.softmax(att, axis=-1)
        out = jnp.einsum('bhfg,bghd->bfhd', att, v).reshape(B, F, H * D)
        res = jnp.einsum('bfe,oe->bfo', x, Wr) + br
        return jax.nn.relu(out + res)
    y = _L0_rec_ref(r_x, L0_rec_Wq, L0_rec_bq, L0_rec_Wk, L0_rec_bk, L0_rec_Wv, L0_rec_bv, L0_rec_Wr, L0_rec_br)
    return y

_drawn_inputs = setup_inputs


def setup_inputs(seed=0):
    import zlib

    import numpy as np

    out = dict(_drawn_inputs(seed))
    spreads = {}
    factors = {'L0_rec_bq': 22.712, 'L0_rec_bk': 64.0}
    for name, (base, spread) in spreads.items():
        noise = np.random.default_rng([zlib.crc32(name.encode()), seed]).standard_normal(out[name].shape)
        drawn = base * np.exp(spread * noise) if base else spread * noise
        out[name] = jnp.asarray(drawn.astype(out[name].dtype))
    for name, factor in factors.items():
        out[name] = (out[name] * factor).astype(out[name].dtype)
    return out
```

```python
import concourse.bass as bass
from concourse import mybir
from contextlib import ExitStack

F32 = mybir.dt.float32
BF16 = mybir.dt.bfloat16
ALU = mybir.AluOpType
ACT = mybir.ActivationFunctionType
AX = mybir.AxisListType


def attention_kernel(nc, x, Wq, bq, Wk, bk, Wv, bv, Wr, br, out):
    BATCH, FIELDS, EMB = x.shape
    OUT = Wq.shape[0]
    HEADS = 4
    DIM = OUT // HEADS
    P = 128
    HALF = 64
    QUAD = 32
    SLOTS = UNITS = PARS = 2
    GROUP = SLOTS * UNITS * PARS
    STEPS = BATCH // GROUP
    HQ = HEADS * FIELDS
    BLOCKS = HQ // QUAD
    GF = UNITS * PARS * FIELDS
    VW = DIM + 1
    SCALE = float(EMB) ** -0.5
    assert OUT == P and EMB == HALF and BATCH % (2 * GROUP) == 0 and HQ % QUAD == 0

    x_in = x.rearrange("(n p us) f e -> n p f us e", p=PARS, us=UNITS * SLOTS)
    y_out = out.rearrange("(n pu s) f c -> n s f pu c", s=SLOTS, pu=PARS * UNITS)

    with ExitStack() as ctx:
        def sb(name, shape, dt=F32):
            return ctx.enter_context(nc.sbuf_tensor(name, shape, dt))

        def sem(name):
            return ctx.enter_context(nc.semaphore(name))

        ident = sb("ident", [P, P])
        neg_ident = sb("neg_ident", [P, QUAD])
        pick_par = sb("pick_par", [P, P], BF16)
        low_part = sb("low_part", [P, 1])
        real_key = sb("real_key", [P, 1])
        w_in = sb("w_in", [P, 4, SLOTS, EMB])
        w_bd = sb("w_bd", [P, 4, SLOTS, P])
        wv_bd = w_bd[:, 2].rearrange("p s c -> p (s c)")
        bias_qk = sb("bias_qk", [P, 2])
        bias_vr = sb("bias_vr", [P, 2, P])
        bias_out = sb("bias_out", [P, P])

        x_rows = sb("x_rows", [P, 2, UNITS, SLOTS, EMB])
        xT = sb("xT", [P, 2, UNITS, PARS, HALF])
        kT = sb("kT", [P, SLOTS, UNITS, PARS, HALF])
        qT_bd = sb("qT_bd", [P, SLOTS, UNITS, PARS, HEADS, FIELDS])
        v_bd = sb("v_bd", [P, UNITS, SLOTS, HEADS, PARS, VW])
        pT = sb("pT", [P, UNITS, SLOTS, HQ])
        m_part = sb("m_part", [P, UNITS, SLOTS * BLOCKS])
        m_swap = sb("m_swap", [P, UNITS, SLOTS * BLOCKS])
        m_full = sb("m_full", [P, UNITS, SLOTS * BLOCKS])
        m_high = sb("m_high", [P, UNITS, SLOTS * BLOCKS], BF16)
        m_split = sb("m_split", [P, UNITS, SLOTS * BLOCKS])
        m_diag = sb("m_diag", [P, UNITS, SLOTS * BLOCKS, QUAD], BF16)
        r_sum = sb("r_sum", [P, UNITS, HEADS * PARS])
        y_att = sb("y_att", [P, UNITS, PARS, HEADS, DIM])
        y_sum = sb("y_sum", [P, UNITS, PARS * OUT])
        y_bias = sb("y_bias", [P, UNITS, PARS, OUT])
        y_rows = sb("y_rows", [P, 2, PARS, UNITS, OUT])  

        st_bank = [ctx.enter_context(nc.psum_tensor(f"st_bank{u}", [P, 512], F32)) for u in range(UNITS)]
        q_bank = ctx.enter_context(nc.psum_tensor("q_bank", [P, 512], F32))
        k_bank = ctx.enter_context(nc.psum_tensor("k_bank", [P, 512], F32))
        vr_bank = [ctx.enter_context(nc.psum_tensor(f"vr_bank{u}", [P, 512], F32)) for u in range(UNITS)]
        o_bank = [ctx.enter_context(nc.psum_tensor(f"o_bank{u}", [P, 512], F32)) for u in range(UNITS)]
        s_ps = [b[:, 0:SLOTS * HQ] for b in st_bank]
        t_ps = [b[:, SLOTS * HQ:SLOTS * HQ + P] for b in st_bank]
        q_ps = q_bank[:, 0:SLOTS * GF]
        k_ps = k_bank[:, 0:SLOTS * GF]
        v_ps = [b[:, 0:SLOTS * OUT] for b in vr_bank]
        r_ps = [b[:, SLOTS * OUT:SLOTS * OUT + PARS * OUT] for b in vr_bank]
        o_ps = [b[:, 0:HEADS * PARS * VW] for b in o_bank]

        consts_loaded = sem("consts_loaded")
        zeroed = sem("zeroed")
        banks_set = sem("banks_set")
        masks_made = sem("masks_made")
        w_turned = sem("w_turned")
        w_placed = sem("w_placed")
        bias_made = sem("bias_made")
        x_loaded = [sem(f"x_loaded{i}") for i in range(2)]
        x_turned = sem("x_turned")
        xT_ready = sem("xT_ready")
        qk_made = sem("qk_made")
        kq_act = sem("kq_act")
        q_dve = sem("q_dve")
        scores_made = sem("scores_made")
        v_made = sem("v_made")
        v_ready = sem("v_ready")
        m_parted = sem("m_parted")
        m_swapped = sem("m_swapped")
        m_done = sem("m_done")
        m_rounded = sem("m_rounded")
        m_ready = sem("m_ready")
        diag_ready = sem("diag_ready")
        shifted = sem("shifted")
        p_ready = sem("p_ready")
        o_made = sem("o_made")
        r_ready = sem("r_ready")
        att_ready = sem("att_ready")
        sum_ready = sem("sum_ready")
        biased = sem("biased")
        y_ready = sem("y_ready")
        y_stored = [sem(f"y_stored{i}") for i in range(2)]

        CONST_DMAS = 4 * SLOTS + 4
        WEIGHT_MASKS = 5
        ALL_MASKS = 22

        def every_group(engine, group, before=None):
            group(0, 0, True, False)
            group(1, 1, False, False)
            with engine.Fori(1, STEPS // 2 - 1) as j:
                group(2 * j, 0, False, False)
                group(2 * j + 1, 1, False, False)
            group(STEPS - 2, 0, False, False)
            group(STEPS - 1, 1, False, True)

        def of_parity(n, parity):
            return n // 2 + 1 if isinstance(n, int) else (n - parity) // 2 + 1

        block = ctx.enter_context(nc.Block())

        @block.sync
        def _(sp):
            for w, src in enumerate((Wq, Wk, Wv, Wr)):
                for s in range(SLOTS):
                    sp.dma_start(w_in[:, w, s, :], src).then_inc(consts_loaded, 16)
            sp.dma_start(bias_qk[:, 0:1], bq.rearrange("(p a) -> p a", a=1)).then_inc(consts_loaded, 16)
            sp.dma_start(bias_qk[:, 1:2], bk.rearrange("(p a) -> p a", a=1)).then_inc(consts_loaded, 16)
            for i, src in enumerate((bv, br)):
                sp.dma_start(bias_vr[:, i, :], src.rearrange("(a c) -> a c", a=1).to_broadcast([P, OUT]))\
                  .then_inc(consts_loaded, 16)

            def load(n, parity):
                for p in range(PARS):
                    sp.dma_start(x_rows[HALF * p:HALF * p + FIELDS, parity].rearrange("f u s e -> f (u s) e"),
                                 x_in[n, p]).then_inc(x_loaded[parity], 16)

            sp.wait_ge(zeroed, 2)
            load(0, 0)
            load(1, 1)

            def group(n, parity, first, last):
                if not (isinstance(n, int) and n >= STEPS - 2):
                    sp.wait_ge(x_turned, UNITS * (n + 1))
                    load(n + 2, parity)
                sp.wait_ge(y_ready, UNITS * (n + 1))
                for s in range(SLOTS):
                    sp.dma_start(y_out[n, s],
                                 y_rows[HALF * s:HALF * s + FIELDS, parity]
                                 .rearrange("f p u c -> f (p u) c")).then_inc(y_stored[parity], 16)

            every_group(sp, group)
            for parity in range(2):
                sp.wait_ge(y_stored[parity], 32 * (STEPS // 2))

        @block.gpsimd
        def _(pool):
            pool.memset(x_rows[:, 0], 0.0).then_inc(zeroed, 1)
            pool.memset(x_rows[:, 1], 0.0).then_inc(zeroed, 1)
            made = 0

            def make(instruction):
                nonlocal made
                made += 1
                instruction.then_inc(masks_made, 1)
                pool.wait_ge(masks_made, made)

            for tile, value in ((xT, 0.0), (ident, 0.0), (neg_ident, 0.0), (w_bd, 0.0)):
                make(pool.memset(tile[:], value))
            make(pool.affine_select(out=ident[:], in_=ident[:], compare_op=ALU.not_equal, fill=1.0, base=0,
                                    pattern=[[-1, P]], channel_multiplier=1))
            assert made == WEIGHT_MASKS
            for tile, value in ((real_key, 1.0), (low_part, 0.0), (pick_par, 0.0), (v_bd, 0.0), (qT_bd, 0.0)):
                make(pool.memset(tile[:], value))
            for g in range(P // QUAD):
                quad = slice(QUAD * g, QUAD * (g + 1))
                make(pool.affine_select(out=neg_ident[quad], in_=neg_ident[quad], compare_op=ALU.not_equal,
                                        fill=-1.0, base=0, pattern=[[-1, QUAD]], channel_multiplier=1))
            for p in range(PARS):
                repeated = slice(HALF * p + QUAD, HALF * (p + 1))
                make(pool.affine_select(out=real_key[repeated], in_=real_key[repeated], compare_op=ALU.is_ge,
                                        fill=0.0, base=FIELDS - QUAD - 1, pattern=[[0, 1]],
                                        channel_multiplier=-1))
                make(pool.memset(low_part[repeated], -1.0))
                make(pool.memset(pick_par[HALF * p:HALF * (p + 1), HALF * p:HALF * (p + 1)], 1.0))
            for p in range(PARS):
                rows = slice(HALF * p, HALF * (p + 1))
                ones = v_bd[rows, :, :, :, p, DIM:VW].rearrange("k u s h a -> k (u s h a)")
                make(pool.tensor_copy(ones, real_key[rows].to_broadcast([HALF, UNITS * SLOTS * HEADS])))
            assert made == ALL_MASKS
            pool.wait_ge(consts_loaded, 16 * CONST_DMAS)
            pool.tensor_tensor(bias_out[:], bias_vr[:, 0], bias_vr[:, 1], ALU.add).then_inc(bias_made, 1)
            pool.wait_ge(bias_made, 1)

            def diagonal(n, u, first):
                pool.wait_ge(m_ready, UNITS * n + u + 1)
                if not first:
                    pool.wait_ge(shifted, UNITS * (n - 1) + u + 1)
                pool.tensor_tensor(m_diag[:, u],
                                   m_split[:, u].unsqueeze(2).to_broadcast([P, SLOTS * BLOCKS, QUAD]),
                                   neg_ident[:].unsqueeze(1).to_broadcast([P, SLOTS * BLOCKS, QUAD]),
                                   ALU.mult).then_inc(diag_ready, 1)

            def finish(n, parity, u):
                pool.wait_ge(sum_ready, UNITS * n + u + 1)
                pool.tensor_tensor(y_bias[:, u], y_sum[:, u].rearrange("r (p c) -> r p c", p=PARS),
                                   bias_out[:].unsqueeze(1).to_broadcast([P, PARS, OUT]), ALU.add)\
                    .then_inc(biased, 1)
                pool.wait_ge(biased, UNITS * n + u + 1)
                if not (isinstance(n, int) and n < 2) and u == 0:
                    pool.wait_ge(y_stored[parity], 32 * (of_parity(n, parity) - 1))
                pool.nop(nofuse=True)
                pool.tensor_scalar(y_rows[:, parity, :, u], y_bias[:, u],
                                   0.0, None, ALU.max).then_inc(y_ready, 1)

            def group(n, parity, first, last):
                for u in range(UNITS):
                    if not first:
                        finish(n - 1, 1 - parity, u)
                    diagonal(n, u, first)
                if last:
                    for u in range(UNITS):
                        finish(n, parity, u)

            every_group(pool, group)

        @block.scalar
        def _(act):
            act.wait_ge(consts_loaded, 16 * CONST_DMAS)
            act.wait_ge(w_turned, 1)
            for w in range(4):
                for s in range(SLOTS):
                    rows = slice(HALF * s, HALF * (s + 1))
                    nc.scalar.copy(w_bd[rows, w, s, :], o_bank[0][rows, w * P:(w + 1) * P]).then_inc(w_placed, 1)

            def project(n, first):
                act.wait_ge(qk_made, n + 1)
                if not first:
                    act.wait_ge(scores_made, UNITS * n)
                k_cols = kT[:].rearrange("d s u p f -> d (s u p) f")
                k_new = k_ps.rearrange("d (b f) -> d b f", f=FIELDS)
                nc.scalar.activation(k_cols[:, :, 0:FIELDS], k_new, ACT.Identity,
                                     bias=bias_qk[:, 1:2]).then_inc(kq_act, 1)
                nc.scalar.activation(k_cols[:, :, FIELDS:HALF], k_new[:, :, 0:HALF - FIELDS], ACT.Identity,
                                     bias=bias_qk[:, 1:2]).then_inc(kq_act, 1)
                nc.scalar.activation(qT_bd[0:DIM, :, :, :, 0, :].rearrange("d s u p f -> d (s u p) f"),
                                     q_ps[0:DIM].rearrange("d (b f) -> d b f", f=FIELDS), ACT.Identity,
                                     bias=bias_qk[0:DIM, 0:1]).then_inc(kq_act, 1)

            def values(n, u, first):
                act.wait_ge(v_made, UNITS * n + u + 1)
                if not first:
                    act.wait_ge(o_made, UNITS * (n - 1) + u + 1)
                for p in range(PARS):
                    rows = slice(HALF * p, HALF * (p + 1))
                    nc.scalar.copy(v_bd[rows, u, :, :, p, 0:DIM].rearrange("k s h d -> k (s h) d"),
                                   v_ps[u][rows].rearrange("k (b d) -> k b d", d=DIM)).then_inc(v_ready, 1)

            def exponentials(n, u, first):
                act.wait_ge(shifted, UNITS * n + u + 1)
                nc.scalar.activation(pT[:, u].rearrange("k s c -> k (s c)"), s_ps[u], ACT.Exp,
                                     scale=SCALE).then_inc(p_ready, 1)

            act.wait_ge(masks_made, ALL_MASKS)
            project(0, True)

            def group(n, parity, first, last):
                values(n, 0, first)
                values(n, 1, first)
                exponentials(n, 0, first)
                exponentials(n, 1, first)
                if not last:
                    project(n + 1, False)

            every_group(act, group)

        @block.vector
        def _(dve):
            for u in range(UNITS):
                nc.vector.memset(vr_bank[u][:], 1.0).then_inc(banks_set, 1)
            nc.vector.memset(o_bank[1][:], 1.0).then_inc(banks_set, 1)
            dve.wait_ge(w_placed, 4 * SLOTS)
            nc.vector.memset(o_bank[0][:], 1.0).then_inc(banks_set, 1)
            dve.wait_ge(consts_loaded, 16 * CONST_DMAS)

            def turn(n, parity, u, wait_free):
                dve.wait_ge(x_turned, UNITS * n + u + 1)
                if not (isinstance(n, int) and n == 0):
                    dve.wait_ge(scores_made, UNITS * (n - 1) + u + 1)
                if wait_free:
                    dve.wait_ge(v_made, UNITS * (n - 1))
                nc.vector.tensor_copy(xT[:, parity, u, :, 0:FIELDS],
                                      t_ps[u].rearrange("e (p f) -> e p f", p=PARS)[:, :, 0:FIELDS])\
                    .then_inc(xT_ready, 1)

            def project(n, first):
                dve.wait_ge(qk_made, n + 1)
                if not first:
                    dve.wait_ge(scores_made, UNITS * n)
                for h in range(1, HEADS):
                    rows = slice(DIM * h, DIM * (h + 1))
                    nc.vector.tensor_scalar(qT_bd[rows, :, :, :, h, :].rearrange("d s u p f -> d (s u p) f"),
                                            q_ps[rows].rearrange("d (b f) -> d b f", f=FIELDS),
                                            bias_qk[rows, 0:1], None, ALU.add).then_inc(q_dve, 1)

            def maxima(n, u):
                c = UNITS * n + u + 1
                dve.wait_ge(scores_made, c)
                nc.vector.tensor_reduce(m_part[:, u], s_ps[u].rearrange("k (b c) -> k b c", c=QUAD),
                                        AX.X, ALU.max, apply_transpose=True).then_inc(m_parted, 1)
                dve.wait_ge(m_parted, c)
                for g in range(P // QUAD):
                    to, of = QUAD * g, QUAD * (g ^ 1)
                    nc.vector.tensor_copy(m_swap[to:to + QUAD, u], m_part[of:of + QUAD, u]).then_inc(m_swapped, 1)
                dve.wait_ge(m_swapped, 4 * c)
                nc.vector.tensor_tensor(m_full[:, u], m_part[:, u], m_swap[:, u], ALU.max).then_inc(m_done, 1)
                dve.wait_ge(m_done, c)
                nc.vector.tensor_copy(m_high[:, u], m_full[:, u]).then_inc(m_rounded, 1)
                dve.wait_ge(m_rounded, c)
                nc.vector.scalar_tensor_tensor(out=m_split[:, u], in0=m_high[:, u], scalar=low_part[:],
                                               in1=m_full[:, u], op0=ALU.mult, op1=ALU.add).then_inc(m_ready, 1)

            def normalise(n, u, first):
                c = UNITS * n + u + 1
                dve.wait_ge(o_made, c)
                o = o_ps[u].rearrange("r (b v) -> r b v", v=VW)
                nc.vector.reciprocal(r_sum[:, u], o[:, :, DIM]).then_inc(r_ready, 1)
                dve.wait_ge(r_ready, c)
                nc.vector.tensor_tensor(y_att[:, u].rearrange("r p h d -> r h p d"),
                                        o_ps[u].rearrange("r (h p v) -> r h p v", p=PARS, v=VW)[:, :, :, 0:DIM],
                                        r_sum[:, u].rearrange("r (h p) -> r h p", p=PARS).unsqueeze(3)
                                        .to_broadcast([P, HEADS, PARS, DIM]),
                                        ALU.mult).then_inc(att_ready, 1)
                dve.wait_ge(att_ready, c)
                if not first:
                    dve.wait_ge(biased, UNITS * (n - 1) + u + 1)
                nc.vector.tensor_tensor(y_sum[:, u], r_ps[u], y_att[:, u].rearrange("r p h d -> r (p h d)"),
                                        ALU.add).then_inc(sum_ready, 1)

            turn(0, 0, 0, False)
            turn(0, 0, 1, False)
            dve.wait_ge(masks_made, ALL_MASKS)
            project(0, True)

            def group(n, parity, first, last):
                for u in range(UNITS):
                    if not first:
                        normalise(n - 1, u, isinstance(n, int) and n == 1)
                    if not last:
                        turn(n + 1, 1 - parity, u, not first)
                    if not first:
                        dve.wait_ge(diag_ready, UNITS * (n - 1) + u + 1)
                    maxima(n, u)
                if not last:
                    project(n + 1, False)
                else:
                    for u in range(UNITS):
                        normalise(n, u, False)

            every_group(dve, group)

        @block.tensor
        def _(pe):
            pe.wait_ge(consts_loaded, 16 * CONST_DMAS)
            pe.wait_ge(masks_made, WEIGHT_MASKS)
            for w in range(4):
                last_one = nc.tensor.transpose(o_bank[0][:, w * P:(w + 1) * P],
                                               w_in[:, w].rearrange("o s e -> o (s e)"), ident[:])
            last_one.then_inc(w_turned, 1)

            def turn(n, parity, u):
                rows = HALF + FIELDS
                nc.tensor.transpose(t_ps[u][:, 0:rows], x_rows[0:rows, parity, u].rearrange("r s e -> r (s e)"),
                                    ident[0:rows, 0:rows]).then_inc(x_turned, 1)

            def project(n, parity):
                pe.wait_ge(xT_ready, UNITS * (n + 1))
                cols = xT[:, parity, :, :, 0:FIELDS].rearrange("e u p f -> e (u p) f")
                for w, ps in enumerate((q_ps, k_ps)):
                    for s in range(SLOTS):
                        mm = nc.tensor.matmul(ps[:, s * GF:(s + 1) * GF], w_bd[:, w, s, :], cols,
                                              start=True, stop=True)
                mm.then_inc(qk_made, 1)

            def scores(n, u):
                for s in range(SLOTS):
                    for p in range(PARS):
                        mm = nc.tensor.matmul(s_ps[u][HALF * p:HALF * (p + 1), s * HQ:(s + 1) * HQ],
                                              kT[:, s, u, p],
                                              qT_bd[:, s, u, p].rearrange("d h f -> d (h f)"),
                                              start=(s == 0), stop=False, skip_group_check=True)
                mm.then_inc(scores_made, 1)

            def values(n, parity, u, first):
                if not first:
                    pe.wait_ge(sum_ready, UNITS * (n - 1) + u + 1)
                nc.tensor.matmul(v_ps[u], xT[:, parity, u].rearrange("e p f -> e (p f)"), wv_bd,
                                 start=True, stop=True)
                for p in range(PARS):
                    for s in range(SLOTS):
                        mm = nc.tensor.matmul(r_ps[u][HALF * s:HALF * s + FIELDS, p * OUT:(p + 1) * OUT],
                                              xT[:, parity, u, p, 0:FIELDS], w_bd[:, 3, s, :], start=True, stop=True)
                mm.then_inc(v_made, 1)

            def shift(n, u):
                pe.wait_ge(diag_ready, UNITS * n + u + 1)
                nc.tensor.matmul(s_ps[u], pick_par[:], m_diag[:, u].rearrange("k b c -> k (b c)"),
                                 start=False, stop=True, skip_group_check=True).then_inc(shifted, 1)

            def attend(n, u):
                pe.wait_ge(p_ready, UNITS * n + u + 1)
                pe.wait_ge(v_ready, 2 * (UNITS * n + u + 1))
                for h in range(HEADS):
                    for s in range(SLOTS):
                        mm = nc.tensor.matmul(o_ps[u][HALF * s:HALF * s + FIELDS, h * PARS * VW:(h + 1) * PARS * VW],
                                              pT[:, u, s, h * FIELDS:(h + 1) * FIELDS],
                                              v_bd[:, u, s, h].rearrange("k p v -> k (p v)"),
                                              start=True, stop=True)
                mm.then_inc(o_made, 1)

            pe.wait_ge(x_loaded[0], 32)
            for u in range(UNITS):
                turn(0, 0, u)
            pe.wait_ge(w_placed, 4 * SLOTS)
            project(0, 0)
            pe.wait_ge(banks_set, 4)

            def group(n, parity, first, last):
                pe.wait_ge(kq_act, 3 * (n + 1))
                pe.wait_ge(q_dve, (HEADS - 1) * (n + 1))
                for u in range(UNITS):
                    if not first:
                        pe.wait_ge(p_ready, UNITS * (n - 1) + u + 1)
                    if not last:
                        if u == 0:
                            pe.wait_ge(x_loaded[1 - parity], 32 * of_parity(n + 1, 1 - parity))
                        turn(n + 1, 1 - parity, u)
                    scores(n, u)
                values(n, parity, 0, first)
                values(n, parity, 1, first)
                shift(n, 0)
                if not last:
                    project(n + 1, 1 - parity)
                shift(n, 1)
                attend(n, 0)
                attend(n, 1)

            every_group(pe, group)


_INS = ["r_x", "L0_rec_Wq", "L0_rec_bq", "L0_rec_Wk", "L0_rec_bk", "L0_rec_Wv", "L0_rec_bv", "L0_rec_Wr", "L0_rec_br"]


def kernel(**inputs):
    import numpy as np
    import concourse.bacc as bacc
    from concourse import mybir as _mybir
    from concourse.bass_utils import run_bass_kernel_spmd

    nc = bacc.Bacc("TRN2", target_bir_lowering=False, num_devices=1)
    arrays, args = {}, []
    for name in _INS:
        a = np.ascontiguousarray(inputs[name])
        arrays[name] = a
        args.append(nc.dram_tensor(name, a.shape, _mybir.dt.from_np(a.dtype), kind="ExternalInput").ap())
    batch, fields, _ = inputs["r_x"].shape
    shape = (batch, fields, inputs["L0_rec_Wq"].shape[0])
    args.append(nc.dram_tensor("y", shape, _mybir.dt.float32, kind="ExternalOutput").ap())
    attention_kernel(nc, *args)
    r = run_bass_kernel_spmd(nc, [arrays], core_ids=[0])
    return r.results[0]["y"]
```

```python
import concourse.bass as bass
from concourse import mybir
from contextlib import ExitStack

F32 = mybir.dt.float32
BF16 = mybir.dt.bfloat16
ALU = mybir.AluOpType
ACT = mybir.ActivationFunctionType
AX = mybir.AxisListType


def attention_kernel(nc, x, Wq, bq, Wk, bk, Wv, bv, Wr, br, out):
    BATCH, FIELDS, EMB = x.shape
    OUT = Wq.shape[0]
    HEADS = 4
    DIM = OUT // HEADS
    P = 128
    HALF = 64
    QUAD = 32
    SLOTS = UNITS = PARS = 2
    GROUP = SLOTS * UNITS * PARS
    STEPS = BATCH // GROUP
    HQ = HEADS * FIELDS
    BLOCKS = HQ // QUAD
    GF = UNITS * PARS * FIELDS
    VW = DIM + 1
    TURN = 4
    SCALE = float(EMB) ** -0.5
    assert OUT == P and EMB == HALF and BATCH % (TURN * GROUP) == 0 and STEPS > 2 * TURN and HQ % QUAD == 0

    x_in = x.rearrange("(n p us) f e -> n p f us e", p=PARS, us=UNITS * SLOTS)
    y_out = out.rearrange("(n pu s) f c -> n s f pu c", s=SLOTS, pu=PARS * UNITS)

    with ExitStack() as ctx:
        def sb(name, shape, dt=F32):
            return ctx.enter_context(nc.sbuf_tensor(name, shape, dt))

        def sem(name):
            return ctx.enter_context(nc.semaphore(name))

        ident = sb("ident", [P, P])
        neg_ident = sb("neg_ident", [P, QUAD])
        pick_par = sb("pick_par", [P, P], BF16)
        low_part = sb("low_part", [P, 1])
        real_key = sb("real_key", [P, 1])
        w_in = sb("w_in", [P, 4, SLOTS, EMB])
        w_bd = sb("w_bd", [P, 4, SLOTS, P])
        wv_bd = w_bd[:, 2].rearrange("p s c -> p (s c)")
        bias_qk = sb("bias_qk", [P, 2])
        bias_vr = sb("bias_vr", [P, 2, P])
        bias_out = sb("bias_out", [P, P])

        x_rows = sb("x_rows", [P, 2, UNITS, SLOTS, EMB])
        xT = sb("xT", [P, TURN, UNITS, PARS, HALF])
        kT = sb("kT", [P, SLOTS, UNITS, PARS, HALF])
        qT_bd = sb("qT_bd", [P, SLOTS, UNITS, PARS, HEADS, FIELDS])
        v_bd = sb("v_bd", [P, UNITS, SLOTS, HEADS, PARS, VW])
        pT = sb("pT", [P, UNITS, SLOTS, HQ])
        m_part = sb("m_part", [P, UNITS, SLOTS * BLOCKS])
        m_swap = sb("m_swap", [P, UNITS, SLOTS * BLOCKS])
        m_full = sb("m_full", [P, UNITS, SLOTS * BLOCKS])
        m_high = sb("m_high", [P, UNITS, SLOTS * BLOCKS], BF16)
        m_split = sb("m_split", [P, UNITS, SLOTS * BLOCKS])
        m_diag = sb("m_diag", [P, UNITS, SLOTS * BLOCKS, QUAD], BF16)
        r_sum = sb("r_sum", [P, UNITS, HEADS * PARS])
        y_att = sb("y_att", [P, UNITS, PARS, HEADS, DIM])
        y_sum = sb("y_sum", [P, UNITS, PARS * OUT])
        y_bias = sb("y_bias", [P, UNITS, PARS, OUT])
        y_rows = sb("y_rows", [P, 2, PARS, UNITS, OUT])  

        st_bank = [ctx.enter_context(nc.psum_tensor(f"st_bank{u}", [P, 512], F32)) for u in range(UNITS)]
        q_bank = ctx.enter_context(nc.psum_tensor("q_bank", [P, 512], F32))
        k_bank = ctx.enter_context(nc.psum_tensor("k_bank", [P, 512], F32))
        vr_bank = [ctx.enter_context(nc.psum_tensor(f"vr_bank{u}", [P, 512], F32)) for u in range(UNITS)]
        o_bank = [ctx.enter_context(nc.psum_tensor(f"o_bank{u}", [P, 512], F32)) for u in range(UNITS)]
        s_ps = [b[:, 0:SLOTS * HQ] for b in st_bank]
        t_ps = [b[:, SLOTS * HQ:SLOTS * HQ + P] for b in st_bank]
        q_ps = q_bank[:, 0:SLOTS * GF]
        k_ps = k_bank[:, 0:SLOTS * GF]
        v_ps = [b[:, 0:SLOTS * OUT] for b in vr_bank]
        r_ps = [b[:, SLOTS * OUT:SLOTS * OUT + PARS * OUT] for b in vr_bank]
        o_ps = [b[:, 0:HEADS * PARS * VW] for b in o_bank]

        consts_loaded = sem("consts_loaded")
        zeroed = sem("zeroed")
        banks_set = sem("banks_set")
        masks_made = sem("masks_made")
        w_turned = sem("w_turned")
        w_placed = sem("w_placed")
        bias_made = sem("bias_made")
        x_loaded = [sem(f"x_loaded{i}") for i in range(2)]
        x_turned = sem("x_turned")
        xT_ready = sem("xT_ready")
        q_made = sem("q_made")
        k_made = sem("k_made")
        kq_act = sem("kq_act")
        q_dve = sem("q_dve")
        scores_made = sem("scores_made")
        v_made = sem("v_made")
        v_ready = sem("v_ready")
        m_parted = sem("m_parted")
        m_swapped = sem("m_swapped")
        m_done = sem("m_done")
        m_ready = sem("m_ready")
        diag_ready = sem("diag_ready")
        shifted = sem("shifted")
        p_ready = sem("p_ready")
        o_made = sem("o_made")
        r_ready = sem("r_ready")
        att_ready = sem("att_ready")
        sum_ready = sem("sum_ready")
        biased = sem("biased")
        y_ready = sem("y_ready")
        y_stored = [sem(f"y_stored{i}") for i in range(2)]

        CONST_DMAS = 4 * SLOTS + 4
        WEIGHT_MASKS = 5
        ALL_MASKS = 22

        def every_group(engine, group):
            for i in range(TURN):
                group(i, i)
            with engine.Fori(1, STEPS // TURN - 1) as turn:
                for i in range(TURN):
                    group(TURN * turn + i, i)
            for i in range(TURN):
                group(STEPS - TURN + i, i)

        def before(n, limit):
            return isinstance(n, int) and n < limit

        def exists(n):
            return not isinstance(n, int) or 0 <= n < STEPS

        def of_parity(n, place):
            return (n - place % 2) // 2 + 1

        block = ctx.enter_context(nc.Block())

        @block.sync
        def _(sp):
            for w, src in enumerate((Wq, Wk, Wv, Wr)):
                for s in range(SLOTS):
                    sp.dma_start(w_in[:, w, s, :], src).then_inc(consts_loaded, 16)
            sp.dma_start(bias_qk[:, 0:1], bq.rearrange("(p a) -> p a", a=1)).then_inc(consts_loaded, 16)
            sp.dma_start(bias_qk[:, 1:2], bk.rearrange("(p a) -> p a", a=1)).then_inc(consts_loaded, 16)
            for i, src in enumerate((bv, br)):
                sp.dma_start(bias_vr[:, i, :], src.rearrange("(a c) -> a c", a=1).to_broadcast([P, OUT]))\
                  .then_inc(consts_loaded, 16)

            def load(n, place):
                parity = place % 2
                for p in range(PARS):
                    sp.dma_start(x_rows[HALF * p:HALF * p + FIELDS, parity].rearrange("f u s e -> f (u s) e"),
                                 x_in[n, p]).then_inc(x_loaded[parity], 16)

            sp.wait_ge(zeroed, 2)
            load(0, 0)
            load(1, 1)

            def store(n, place):
                parity = place % 2
                sp.wait_ge(y_ready, UNITS * (n + 1))
                for s in range(SLOTS):
                    sp.dma_start(y_out[n, s], y_rows[HALF * s:HALF * s + FIELDS, parity]
                                 .rearrange("f p u c -> f (p u) c")).then_inc(y_stored[parity], 16)

            def group(n, place):
                if exists(n + 4):
                    sp.wait_ge(x_turned, UNITS * (n + 3))
                    load(n + 4, place)
                if not before(n, 1):
                    store(n - 1, place + 1)

            for n in (2, 3):
                sp.wait_ge(x_turned, UNITS * (n - 1))
                load(n, n)
            every_group(sp, group)
            store(STEPS - 1, STEPS - 1)
            for parity in range(2):
                sp.wait_ge(y_stored[parity], 32 * (STEPS // 2))

        @block.gpsimd
        def _(pool):
            pool.memset(x_rows[:, 0], 0.0).then_inc(zeroed, 1)
            pool.memset(x_rows[:, 1], 0.0).then_inc(zeroed, 1)
            made = 0

            def make(instruction):
                nonlocal made
                made += 1
                instruction.then_inc(masks_made, 1)
                pool.wait_ge(masks_made, made)

            for tile, value in ((xT, 0.0), (ident, 0.0), (neg_ident, 0.0), (w_bd, 0.0)):
                make(pool.memset(tile[:], value))
            make(pool.affine_select(out=ident[:], in_=ident[:], compare_op=ALU.not_equal, fill=1.0, base=0,
                                    pattern=[[-1, P]], channel_multiplier=1))
            assert made == WEIGHT_MASKS
            for tile, value in ((real_key, 1.0), (low_part, 0.0), (pick_par, 0.0), (v_bd, 0.0), (qT_bd, 0.0)):
                make(pool.memset(tile[:], value))
            for g in range(P // QUAD):
                quad = slice(QUAD * g, QUAD * (g + 1))
                make(pool.affine_select(out=neg_ident[quad], in_=neg_ident[quad], compare_op=ALU.not_equal,
                                        fill=-1.0, base=0, pattern=[[-1, QUAD]], channel_multiplier=1))
            for p in range(PARS):
                repeated = slice(HALF * p + QUAD, HALF * (p + 1))
                make(pool.affine_select(out=real_key[repeated], in_=real_key[repeated], compare_op=ALU.is_ge,
                                        fill=0.0, base=FIELDS - QUAD - 1, pattern=[[0, 1]],
                                        channel_multiplier=-1))
                make(pool.memset(low_part[repeated], -1.0))
                make(pool.memset(pick_par[HALF * p:HALF * (p + 1), HALF * p:HALF * (p + 1)], 1.0))
            for p in range(PARS):
                rows = slice(HALF * p, HALF * (p + 1))
                ones = v_bd[rows, :, :, :, p, DIM:VW].rearrange("k u s h a -> k (u s h a)")
                make(pool.tensor_copy(ones, real_key[rows].to_broadcast([HALF, UNITS * SLOTS * HEADS])))
            assert made == ALL_MASKS
            pool.wait_ge(consts_loaded, 16 * CONST_DMAS)
            pool.tensor_tensor(bias_out[:], bias_vr[:, 0], bias_vr[:, 1], ALU.add).then_inc(bias_made, 1)
            pool.wait_ge(bias_made, 1)

            def diagonal(n, u):
                pool.wait_ge(m_ready, UNITS * n + u + 1)
                pool.tensor_tensor(m_diag[:, u],
                                   m_split[:, u].unsqueeze(2).to_broadcast([P, SLOTS * BLOCKS, QUAD]),
                                   neg_ident[:].unsqueeze(1).to_broadcast([P, SLOTS * BLOCKS, QUAD]),
                                   ALU.mult).then_inc(diag_ready, 1)

            def add_bias(n, u):
                pool.wait_ge(sum_ready, UNITS * n + u + 1)
                pool.tensor_tensor(y_bias[:, u], y_sum[:, u].rearrange("r (p c) -> r p c", p=PARS),
                                   bias_out[:].unsqueeze(1).to_broadcast([P, PARS, OUT]), ALU.add)\
                    .then_inc(biased, 1)

            def relu(n, place, u):
                if not before(n, 2):
                    pool.wait_ge(y_stored[place % 2], 32 * (of_parity(n, place) - 1))
                pool.wait_ge(biased, UNITS * n + u + 1)
                pool.nop(nofuse=True)
                pool.tensor_scalar(y_rows[:, place % 2, :, u], y_bias[:, u],
                                   0.0, None, ALU.max).then_inc(y_ready, 1)

            def group(n, place):
                if not before(n, 1):
                    add_bias(n - 1, 0)
                    relu(n - 1, place + 1, 0)
                diagonal(n, 0)
                if not before(n, 1):
                    add_bias(n - 1, 1)
                diagonal(n, 1)
                if not before(n, 1):
                    relu(n - 1, place + 1, 1)

            every_group(pool, group)
            for u in range(UNITS):
                add_bias(STEPS - 1, u)
                relu(STEPS - 1, STEPS - 1, u)

        @block.scalar
        def _(act):
            act.wait_ge(consts_loaded, 16 * CONST_DMAS)
            act.wait_ge(w_turned, 1)
            for w in range(4):
                for s in range(SLOTS):
                    rows = slice(HALF * s, HALF * (s + 1))
                    nc.scalar.copy(w_bd[rows, w, s, :], o_bank[0][rows, w * P:(w + 1) * P]).then_inc(w_placed, 1)

            def queries(n):
                act.wait_ge(q_made, n + 1)
                for h in range(2):
                    rows = slice(DIM * h, DIM * (h + 1))
                    nc.scalar.activation(qT_bd[rows, :, :, :, h, :].rearrange("d s u p f -> d (s u p) f"),
                                         q_ps[rows].rearrange("d (b f) -> d b f", f=FIELDS), ACT.Identity,
                                         bias=bias_qk[rows, 0:1]).then_inc(kq_act, 1)

            def keys(n):
                act.wait_ge(k_made, n + 1)
                k_cols = kT[:].rearrange("d s u p f -> d (s u p) f")
                k_new = k_ps.rearrange("d (b f) -> d b f", f=FIELDS)
                nc.scalar.activation(k_cols[:, :, 0:FIELDS], k_new, ACT.Identity,
                                     bias=bias_qk[:, 1:2]).then_inc(kq_act, 1)
                nc.scalar.activation(k_cols[:, :, FIELDS:HALF], k_new[:, :, 0:HALF - FIELDS], ACT.Identity,
                                     bias=bias_qk[:, 1:2]).then_inc(kq_act, 1)

            def values(n, u):
                act.wait_ge(v_made, UNITS * n + u + 1)
                for p in range(PARS):
                    rows = slice(HALF * p, HALF * (p + 1))
                    nc.scalar.copy(v_bd[rows, u, :, :, p, 0:DIM].rearrange("k s h d -> k (s h) d"),
                                   v_ps[u][rows].rearrange("k (b d) -> k b d", d=DIM)).then_inc(v_ready, 1)

            def exponentials(n, u):
                act.wait_ge(shifted, UNITS * n + u + 1)
                nc.scalar.activation(pT[:, u].rearrange("k s c -> k (s c)"), s_ps[u], ACT.Exp,
                                     scale=SCALE).then_inc(p_ready, 1)

            act.wait_ge(masks_made, ALL_MASKS)
            queries(0)
            keys(0)

            def group(n, place):
                if not before(n, 1):
                    exponentials(n - 1, 1)
                values(n, 0)
                if exists(n + 1):
                    queries(n + 1)
                exponentials(n, 0)
                if exists(n + 1):
                    keys(n + 1)
                values(n, 1)

            every_group(act, group)
            exponentials(STEPS - 1, 1)

        @block.vector
        def _(dve):
            for u in range(UNITS):
                nc.vector.memset(vr_bank[u][:], 1.0).then_inc(banks_set, 1)
            nc.vector.memset(o_bank[1][:], 1.0).then_inc(banks_set, 1)
            dve.wait_ge(w_placed, 4 * SLOTS)
            nc.vector.memset(o_bank[0][:], 1.0).then_inc(banks_set, 1)
            dve.wait_ge(consts_loaded, 16 * CONST_DMAS)

            def turn(n, place, u):
                dve.wait_ge(x_turned, UNITS * n + u + 1)
                if not before(n, 2):
                    dve.wait_ge(scores_made, UNITS * (n - 2) + u + 1)
                nc.vector.tensor_copy(xT[:, place % TURN, u, :, 0:FIELDS],
                                      t_ps[u].rearrange("e (p f) -> e p f", p=PARS)[:, :, 0:FIELDS])\
                    .then_inc(xT_ready, 1)

            def queries(n):
                dve.wait_ge(q_made, n + 1)
                for h in range(2, HEADS):
                    rows = slice(DIM * h, DIM * (h + 1))
                    nc.vector.tensor_scalar(qT_bd[rows, :, :, :, h, :].rearrange("d s u p f -> d (s u p) f"),
                                            q_ps[rows].rearrange("d (b f) -> d b f", f=FIELDS),
                                            bias_qk[rows, 0:1], None, ALU.add).then_inc(q_dve, 1)

            def max_of_quadrant(n, u):
                dve.wait_ge(scores_made, UNITS * n + u + 1)
                nc.vector.tensor_reduce(m_part[:, u], s_ps[u].rearrange("k (b c) -> k b c", c=QUAD),
                                        AX.X, ALU.max, apply_transpose=True).then_inc(m_parted, 1)

            def max_of_keys(n, u):
                c = UNITS * n + u + 1
                dve.wait_ge(m_parted, c)
                for g in range(P // QUAD):
                    to, of = QUAD * g, QUAD * (g ^ 1)
                    nc.vector.tensor_copy(m_swap[to:to + QUAD, u], m_part[of:of + QUAD, u]).then_inc(m_swapped, 1)
                dve.wait_ge(m_swapped, 4 * c)
                nc.vector.tensor_tensor(m_full[:, u], m_part[:, u], m_swap[:, u], ALU.max).then_inc(m_done, 1)
                nc.vector.tensor_tensor(m_high[:, u], m_part[:, u], m_swap[:, u], ALU.max).then_inc(m_done, 1)

            def max_in_parts(n, u):
                c = UNITS * n + u + 1
                dve.wait_ge(m_done, 2 * c)
                if not before(n, 1):
                    dve.wait_ge(diag_ready, UNITS * (n - 1) + u + 1)
                nc.vector.scalar_tensor_tensor(out=m_split[:, u], in0=m_high[:, u], scalar=low_part[:],
                                               in1=m_full[:, u], op0=ALU.mult, op1=ALU.add).then_inc(m_ready, 1)

            def reciprocals(n, u):
                dve.wait_ge(o_made, UNITS * n + u + 1)
                o = o_ps[u].rearrange("r (b v) -> r b v", v=VW)
                nc.vector.reciprocal(r_sum[:, u], o[:, :, DIM]).then_inc(r_ready, 1)

            def normalise(n, u):
                dve.wait_ge(r_ready, UNITS * n + u + 1)
                nc.vector.tensor_tensor(y_att[:, u].rearrange("r p h d -> r h p d"),
                                        o_ps[u].rearrange("r (h p v) -> r h p v", p=PARS, v=VW)[:, :, :, 0:DIM],
                                        r_sum[:, u].rearrange("r (h p) -> r h p", p=PARS).unsqueeze(3)
                                        .to_broadcast([P, HEADS, PARS, DIM]),
                                        ALU.mult).then_inc(att_ready, 1)

            def add_residual(n, u):
                dve.wait_ge(att_ready, UNITS * n + u + 1)
                if not before(n, 1):
                    dve.wait_ge(biased, UNITS * (n - 1) + u + 1)
                nc.vector.tensor_tensor(y_sum[:, u], r_ps[u], y_att[:, u].rearrange("r p h d -> r (p h d)"),
                                        ALU.add).then_inc(sum_ready, 1)

            for n in range(2):
                for u in range(UNITS):
                    turn(n, n, u)
                if n == 0:
                    dve.wait_ge(masks_made, ALL_MASKS)
                    queries(0)

            def group(n, place):
                if not before(n, 1):
                    reciprocals(n - 1, 0)
                    normalise(n - 1, 0)
                    add_residual(n - 1, 0)
                max_of_quadrant(n, 0)
                if exists(n + 2):
                    turn(n + 2, place + 2, 0)
                max_of_keys(n, 0)
                if not before(n, 1):
                    reciprocals(n - 1, 1)
                max_in_parts(n, 0)
                if not before(n, 1):
                    normalise(n - 1, 1)
                max_of_quadrant(n, 1)
                if not before(n, 1):
                    add_residual(n - 1, 1)
                max_of_keys(n, 1)
                if exists(n + 2):
                    turn(n + 2, place + 2, 1)
                max_in_parts(n, 1)
                if exists(n + 1):
                    queries(n + 1)

            every_group(dve, group)
            for u in range(UNITS):
                reciprocals(STEPS - 1, u)
                normalise(STEPS - 1, u)
                add_residual(STEPS - 1, u)

        @block.tensor
        def _(pe):
            pe.wait_ge(consts_loaded, 16 * CONST_DMAS)
            pe.wait_ge(masks_made, WEIGHT_MASKS)
            for w in range(4):
                last_one = nc.tensor.transpose(o_bank[0][:, w * P:(w + 1) * P],
                                               w_in[:, w].rearrange("o s e -> o (s e)"), ident[:])
            last_one.then_inc(w_turned, 1)

            def turn(n, place, u):
                rows = HALF + FIELDS
                nc.tensor.transpose(t_ps[u][:, 0:rows], x_rows[0:rows, place % 2, u].rearrange("r s e -> r (s e)"),
                                    ident[0:rows, 0:rows]).then_inc(x_turned, 1)

            def project(n, place):
                pe.wait_ge(xT_ready, UNITS * (n + 1))
                cols = xT[:, place % TURN, :, :, 0:FIELDS].rearrange("e u p f -> e (u p) f")
                for w, (ps, made) in enumerate(((q_ps, q_made), (k_ps, k_made))):
                    for s in range(SLOTS):
                        mm = nc.tensor.matmul(ps[:, s * GF:(s + 1) * GF], w_bd[:, w, s, :], cols,
                                              start=True, stop=True)
                    mm.then_inc(made, 1)

            def scores(n, u):
                for s in range(SLOTS):
                    for p in range(PARS):
                        mm = nc.tensor.matmul(s_ps[u][HALF * p:HALF * (p + 1), s * HQ:(s + 1) * HQ],
                                              kT[:, s, u, p],
                                              qT_bd[:, s, u, p].rearrange("d h f -> d (h f)"),
                                              start=(s == 0), stop=False, skip_group_check=True)
                mm.then_inc(scores_made, 1)

            def values(n, place, u):
                if not before(n, 1):
                    pe.wait_ge(sum_ready, UNITS * (n - 1) + u + 1)
                nc.tensor.matmul(v_ps[u], xT[:, place, u].rearrange("e p f -> e (p f)"), wv_bd,
                                 start=True, stop=True)
                for p in range(PARS):
                    for s in range(SLOTS):
                        mm = nc.tensor.matmul(r_ps[u][HALF * s:HALF * s + FIELDS, p * OUT:(p + 1) * OUT],
                                              xT[:, place, u, p, 0:FIELDS], w_bd[:, 3, s, :], start=True, stop=True)
                mm.then_inc(v_made, 1)

            def shift(n, u):
                pe.wait_ge(diag_ready, UNITS * n + u + 1)
                nc.tensor.matmul(s_ps[u], pick_par[:], m_diag[:, u].rearrange("k b c -> k (b c)"),
                                 start=False, stop=True, skip_group_check=True).then_inc(shifted, 1)

            def attend(n, u):
                pe.wait_ge(p_ready, UNITS * n + u + 1)
                pe.wait_ge(v_ready, 2 * (UNITS * n + u + 1))
                for h in range(HEADS):
                    for s in range(SLOTS):
                        mm = nc.tensor.matmul(o_ps[u][HALF * s:HALF * s + FIELDS, h * PARS * VW:(h + 1) * PARS * VW],
                                              pT[:, u, s, h * FIELDS:(h + 1) * FIELDS],
                                              v_bd[:, u, s, h].rearrange("k p v -> k (p v)"),
                                              start=True, stop=True)
                mm.then_inc(o_made, 1)

            for n in range(2):
                pe.wait_ge(x_loaded[n], 32)
                if n == 1:
                    pe.wait_ge(xT_ready, UNITS)
                for u in range(UNITS):
                    turn(n, n, u)
            pe.wait_ge(w_placed, 4 * SLOTS)
            project(0, 0)
            pe.wait_ge(banks_set, 4)
            pe.wait_ge(xT_ready, 2 * UNITS)

            def turn_and_scores(n, place, u):
                if not before(n, 1):
                    pe.wait_ge(p_ready, UNITS * (n - 1) + u + 1)
                if exists(n + 2):
                    if u == 0:
                        pe.wait_ge(x_loaded[place % 2], 32 * of_parity(n + 2, place))
                    turn(n + 2, place + 2, u)
                scores(n, u)

            def group(n, place):
                pe.wait_ge(kq_act, 4 * (n + 1))
                pe.wait_ge(q_dve, 2 * (n + 1))
                turn_and_scores(n, place, 0)
                if not before(n, 1):
                    attend(n - 1, 1)
                turn_and_scores(n, place, 1)
                values(n, place, 0)
                if exists(n + 1):
                    project(n + 1, place + 1)
                shift(n, 0)
                values(n, place, 1)
                attend(n, 0)
                shift(n, 1)

            every_group(pe, group)
            attend(STEPS - 1, 1)


_INS = ["r_x", "L0_rec_Wq", "L0_rec_bq", "L0_rec_Wk", "L0_rec_bk", "L0_rec_Wv", "L0_rec_bv", "L0_rec_Wr", "L0_rec_br"]


def kernel(**inputs):
    import numpy as np
    import concourse.bacc as bacc
    from concourse import mybir as _mybir
    from concourse.bass_utils import run_bass_kernel_spmd

    nc = bacc.Bacc("TRN2", target_bir_lowering=False, num_devices=1)
    arrays, args = {}, []
    for name in _INS:
        a = np.ascontiguousarray(inputs[name])
        arrays[name] = a
        args.append(nc.dram_tensor(name, a.shape, _mybir.dt.from_np(a.dtype), kind="ExternalInput").ap())
    batch, fields, _ = inputs["r_x"].shape
    shape = (batch, fields, inputs["L0_rec_Wq"].shape[0])
    args.append(nc.dram_tensor("y", shape, _mybir.dt.float32, kind="ExternalOutput").ap())
    attention_kernel(nc, *args)
    r = run_bass_kernel_spmd(nc, [arrays], core_ids=[0])
    return r.results[0]["y"]
```

```python
import concourse.bass as bass
from concourse import mybir
from contextlib import ExitStack

F32 = mybir.dt.float32
F32R = mybir.dt.float32r
BF16 = mybir.dt.bfloat16
ALU = mybir.AluOpType
ACT = mybir.ActivationFunctionType
AX = mybir.AxisListType


def attention_kernel(nc, x, Wq, bq, Wk, bk, Wv, bv, Wr, br, out):
    BATCH, FIELDS, EMB = x.shape
    OUT = Wq.shape[0]
    HEADS = 4
    DIM = OUT // HEADS
    P = 128
    HALF = 64
    QUAD = 32
    SLOTS = UNITS = PARS = 2
    GROUP = SLOTS * UNITS * PARS
    STEPS = BATCH // GROUP
    HQ = HEADS * FIELDS
    BLOCKS = HQ // QUAD
    GF = UNITS * PARS * FIELDS
    VW = DIM + 1
    TURN = 8
    SPLITS = 4
    ACT_HEADS = 3
    SCALE = float(EMB) ** -0.5
    assert OUT == P and EMB == HALF and BATCH % (TURN * GROUP) == 0 and STEPS > 2 * TURN and HQ % QUAD == 0

    x_in = x.rearrange("(n p us) f e -> n p f us e", p=PARS, us=UNITS * SLOTS)
    y_out = out.rearrange("(n pu s) f c -> n s f pu c", s=SLOTS, pu=PARS * UNITS)

    with ExitStack() as ctx:
        def sb(name, shape, dt=F32):
            return ctx.enter_context(nc.sbuf_tensor(name, shape, dt))

        def sem(name):
            return ctx.enter_context(nc.semaphore(name))

        ident = sb("ident", [P, P])
        neg_ident = sb("neg_ident", [P, QUAD])
        pick_par = sb("pick_par", [P, P], BF16)
        real_key = sb("real_key", [P, 1])
        w_in = sb("w_in", [P, 4, 2, EMB])
        w_high = sb("w_high", [P, 4, OUT], F32R)
        w_low = sb("w_low", [P, 4, OUT], F32R)
        biases = sb("biases", [P, 4])
        out_bias = sb("out_bias", [P, 1])

        x_rows = sb("x_rows", [P, 2, UNITS, SLOTS, EMB])
        xT = sb("xT", [P, 2, UNITS, PARS, FIELDS])
        x_split = sb("x_split", [P, SPLITS, SLOTS, UNITS, PARS, FIELDS], F32R)
        kT = sb("kT", [P, 2, SLOTS, UNITS, PARS, HALF])
        qT_bd = sb("qT_bd", [P, 2, SLOTS, UNITS, PARS, HEADS, FIELDS])
        vT = sb("vT", [P, 2, UNITS, SLOTS, PARS, HALF])
        rT = sb("rT", [P, 2, UNITS, PARS, SLOTS, HALF])
        v_bd = sb("v_bd", [P, UNITS, SLOTS, HEADS, PARS, VW])
        pT = sb("pT", [P, UNITS, SLOTS, HQ])
        m_part = sb("m_part", [P, UNITS, SLOTS * BLOCKS])
        m_swap = sb("m_swap", [P, UNITS, SLOTS * BLOCKS])
        m_high = sb("m_high", [P, UNITS, SLOTS * BLOCKS], BF16)
        m_split = sb("m_split", [P, UNITS, SLOTS * BLOCKS])
        m_diag = sb("m_diag", [P, UNITS, SLOTS * BLOCKS, QUAD], BF16)
        r_sum = sb("r_sum", [P, UNITS, HEADS * PARS])
        y_att = sb("y_att", [P, UNITS, PARS, HEADS, DIM])
        y_sum = sb("y_sum", [P, UNITS, PARS * OUT])
        y_rows = sb("y_rows", [P, 2, PARS, UNITS, OUT])

        st_bank = [ctx.enter_context(nc.psum_tensor(f"st_bank{u}", [P, 512], F32)) for u in range(UNITS)]
        q_bank = ctx.enter_context(nc.psum_tensor("q_bank", [P, 512], F32))
        k_bank = ctx.enter_context(nc.psum_tensor("k_bank", [P, 512], F32))
        vr_bank = [ctx.enter_context(nc.psum_tensor(f"vr_bank{u}", [P, 512], F32)) for u in range(UNITS)]
        o_bank = [ctx.enter_context(nc.psum_tensor(f"o_bank{u}", [P, 512], F32)) for u in range(UNITS)]
        s_ps = [b[:, 0:SLOTS * HQ] for b in st_bank]
        t_ps = [b[:, SLOTS * HQ:SLOTS * HQ + P] for b in st_bank]
        q_ps = vT_ps = q_bank[:, 0:SLOTS * GF]
        k_ps = rT_ps = k_bank[:, 0:SLOTS * GF]
        v_ps = [b[:, 0:SLOTS * OUT] for b in vr_bank]
        r_ps = [b[:, SLOTS * OUT:SLOTS * OUT + PARS * OUT] for b in vr_bank]
        o_ps = [b[:, 0:HEADS * PARS * VW] for b in o_bank]

        w_loaded = sem("w_loaded")
        biases_loaded = sem("biases_loaded")
        biases_added = sem("biases_added")
        zeroed = sem("zeroed")
        banks_set = sem("banks_set")
        cleared = sem("cleared")
        masks_made = sem("masks_made")
        w_turned = sem("w_turned")
        w_rounded = sem("w_rounded")
        w_split = sem("w_split")
        x_loaded = [sem(f"x_loaded{i}") for i in range(2)]
        x_turned = sem("x_turned")
        xT_ready = sem("xT_ready")
        x_rounded = sem("x_rounded")
        x_lowered = sem("x_lowered")
        q_made = sem("q_made")
        k_made = sem("k_made")
        k_ready = sem("k_ready")
        k_again = sem("k_again")
        q_act = sem("q_act")
        q_dve = sem("q_dve")
        vT_made = sem("vT_made")
        rT_made = sem("rT_made")
        vrT_ready = sem("vrT_ready")
        scores_made = sem("scores_made")
        v_made = sem("v_made")
        v_ready = sem("v_ready")
        m_parted = sem("m_parted")
        m_swapped = sem("m_swapped")
        m_done = sem("m_done")
        m_ready = sem("m_ready")
        diag_ready = sem("diag_ready")
        shifted = sem("shifted")
        p_ready = sem("p_ready")
        o_made = sem("o_made")
        r_ready = sem("r_ready")
        att_ready = sem("att_ready")
        sum_ready = sem("sum_ready")
        y_ready = sem("y_ready")
        y_stored = [sem(f"y_stored{i}") for i in range(2)]

        WEIGHT_MASKS = 2
        ALL_MASKS = 18

        def every_group(engine, group):
            for i in range(TURN):
                group(i, i)
            with engine.Fori(1, STEPS // TURN - 1) as turn:
                for i in range(TURN):
                    group(TURN * turn + i, i)
            for i in range(TURN):
                group(STEPS - TURN + i, i)

        def before(n, limit):
            return isinstance(n, int) and n < limit

        def exists(n):
            return not isinstance(n, int) or 0 <= n < STEPS

        def of_parity(n, place):
            return (n - place % 2) // 2 + 1

        block = ctx.enter_context(nc.Block())

        @block.sync
        def _(sp):
            for w, weight in enumerate((Wq, Wk, Wv, Wr)):
                sp.dma_start(w_in[:, w], weight.unsqueeze(1).to_broadcast([P, 2, EMB])).then_inc(w_loaded, 16)

            def load(n, place):
                parity = place % 2
                for p in range(PARS):
                    sp.dma_start(x_rows[HALF * p:HALF * p + FIELDS, parity].rearrange("f u s e -> f (u s) e"),
                                 x_in[n, p]).then_inc(x_loaded[parity], 16)

            sp.wait_ge(zeroed, 2)
            load(0, 0)
            load(1, 1)
            for w, bias in enumerate((bq, bk, bv, br)):
                sp.dma_start(biases[:, w:w + 1], bias.rearrange("(p a) -> p a", a=1)).then_inc(biases_loaded, 16)

            def store(n, place):
                parity = place % 2
                sp.wait_ge(y_ready, UNITS * (n + 1))
                for s in range(SLOTS):
                    sp.dma_start(y_out[n, s], y_rows[HALF * s:HALF * s + FIELDS, parity]
                                 .rearrange("f p u c -> f (p u) c")).then_inc(y_stored[parity], 16)

            def group(n, place):
                if exists(n + 4):
                    sp.wait_ge(x_turned, UNITS * (n + 3))
                    load(n + 4, place)
                if not before(n, 2):
                    store(n - 2, place + 2)

            for n in (2, 3):
                sp.wait_ge(x_turned, UNITS * (n - 1))
                load(n, n)
            every_group(sp, group)
            for n in (STEPS - 2, STEPS - 1):
                store(n, n)
            for parity in range(2):
                sp.wait_ge(y_stored[parity], 32 * (STEPS // 2))

        @block.gpsimd
        def _(pool):
            pool.memset(x_rows[:, 0], 0.0).then_inc(zeroed, 1)
            pool.memset(x_rows[:, 1], 0.0).then_inc(zeroed, 1)
            made = 0

            def make(instruction):
                nonlocal made
                made += 1
                instruction.then_inc(masks_made, 1)
                pool.wait_ge(masks_made, made)

            make(pool.memset(ident[:], 0.0))
            make(pool.affine_select(out=ident[:], in_=ident[:], compare_op=ALU.not_equal, fill=1.0, base=0,
                                    pattern=[[-1, P]], channel_multiplier=1))
            assert made == WEIGHT_MASKS
            for tile, value in ((neg_ident, 0.0), (real_key, 1.0), (m_swap, 0.0), (pick_par, 0.0), (rT, 0.0),
                                (v_bd, 0.0)):
                make(pool.memset(tile[:], value))
            for g in range(P // QUAD):
                quad = slice(QUAD * g, QUAD * (g + 1))
                make(pool.affine_select(out=neg_ident[quad], in_=neg_ident[quad], compare_op=ALU.not_equal,
                                        fill=-1.0, base=0, pattern=[[-1, QUAD]], channel_multiplier=1))
            for p in range(PARS):
                repeated = slice(HALF * p + QUAD, HALF * (p + 1))
                make(pool.affine_select(out=real_key[repeated], in_=real_key[repeated], compare_op=ALU.is_ge,
                                        fill=0.0, base=FIELDS - QUAD - 1, pattern=[[0, 1]],
                                        channel_multiplier=-1))
                make(pool.memset(pick_par[HALF * p:HALF * (p + 1), HALF * p:HALF * (p + 1)], 1.0))
            for p in range(PARS):
                rows = slice(HALF * p, HALF * (p + 1))
                ones = v_bd[rows, :, :, :, p, DIM:VW].rearrange("k u s h a -> k (u s h a)")
                make(pool.tensor_copy(ones, real_key[rows].to_broadcast([HALF, UNITS * SLOTS * HEADS])))
            assert made == ALL_MASKS

            def diagonal(n, u):
                pool.wait_ge(m_ready, 2 * (UNITS * n + u + 1))
                pool.tensor_tensor(m_diag[:, u],
                                   m_split[:, u].unsqueeze(2).to_broadcast([P, SLOTS * BLOCKS, QUAD]),
                                   neg_ident[:].unsqueeze(1).to_broadcast([P, SLOTS * BLOCKS, QUAD]),
                                   ALU.mult).then_inc(diag_ready, 1)

            def relu(n, place, u):
                if not before(n, 2):
                    pool.wait_ge(y_stored[place % 2], 32 * (of_parity(n, place) - 1))
                pool.wait_ge(sum_ready, UNITS * n + u + 1)
                pool.nop(nofuse=True)
                pool.tensor_scalar(y_rows[:, place % 2, :, u], y_sum[:, u].rearrange("r (p c) -> r p c", p=PARS),
                                   0.0, None, ALU.max).then_inc(y_ready, 1)

            def lower(n, place):
                pool.wait_ge(x_rounded, SLOTS * (n + 1))
                for s in range(SLOTS):
                    rows, other = slice(HALF * s, HALF * (s + 1)), slice(HALF * (1 - s), HALF * (2 - s))
                    pool.tensor_tensor(x_split[other, place % SPLITS, s].rearrange("e u p f -> e (u p f)"),
                                       xT[rows, place % 2].rearrange("e u p f -> e (u p f)"),
                                       x_split[rows, place % SPLITS, s].rearrange("e u p f -> e (u p f)").bitcast(F32),
                                       ALU.subtract).then_inc(x_lowered, 1)
                    pool.wait_ge(x_lowered, SLOTS * n + s + 1)

            def group(n, place):
                diagonal(n, 0)
                if exists(n + 2):
                    pool.wait_ge(diag_ready, UNITS * n + 1)
                    if not before(n, 2):
                        pool.wait_ge(y_ready, UNITS * (n - 2) + 1)
                    lower(n + 2, place + 2)
                if not before(n, 2):
                    relu(n - 2, place + 2, 1)
                diagonal(n, 1)
                if not before(n, 1):
                    relu(n - 1, place + 1, 0)

            for n in range(2):
                lower(n, n)
            every_group(pool, group)
            relu(STEPS - 2, STEPS - 2, 1)
            for u in range(UNITS):
                relu(STEPS - 1, STEPS - 1, u)

        @block.scalar
        def _(act):
            act.wait_ge(w_turned, 1)
            nc.scalar.copy(w_high[:].rearrange("e w c -> e (w c)"), o_bank[0][:]).then_inc(w_rounded, 1)

            def round_x(n, place):
                act.wait_ge(xT_ready, UNITS * (n + 1))
                for s in range(SLOTS):
                    rows = slice(HALF * s, HALF * (s + 1))
                    nc.scalar.copy(x_split[rows, place % SPLITS, s].rearrange("e u p f -> e (u p f)"),
                                   xT[rows, place % 2].rearrange("e u p f -> e (u p f)")).then_inc(x_rounded, 1)

            def queries(n, place):
                act.wait_ge(q_made, n + 1)
                for h in range(ACT_HEADS):
                    rows = slice(DIM * h, DIM * (h + 1))
                    nc.scalar.activation(qT_bd[rows, place % 2, :, :, :, h, :].rearrange("d s u p f -> d (s u p) f"),
                                         q_ps[rows].rearrange("d (b f) -> d b f", f=FIELDS), ACT.Identity,
                                         bias=biases[rows, 0:1]).then_inc(q_act, 1)

            def keys(n, place):
                act.wait_ge(k_made, n + 1)
                nc.scalar.activation(kT[:, place % 2].rearrange("d s u p f -> d (s u p) f")[:, :, 0:FIELDS],
                                     k_ps.rearrange("d (b f) -> d b f", f=FIELDS), ACT.Identity,
                                     bias=biases[:, 1:2]).then_inc(k_ready, 1)

            def values_T(n, place):
                act.wait_ge(vT_made, n + 1)
                nc.scalar.copy(vT[:, place % 2].rearrange("d u s p f -> d (u s p) f")[:, :, 0:FIELDS],
                               vT_ps.rearrange("d (b f) -> d b f", f=FIELDS)).then_inc(vrT_ready, 1)

            def residual_T(n, place):
                act.wait_ge(rT_made, n + 1)
                nc.scalar.activation(rT[:, place % 2].rearrange("d u p s f -> d (u p s) f")[:, :, 0:FIELDS],
                                     rT_ps.rearrange("d (b f) -> d b f", f=FIELDS), ACT.Identity,
                                     bias=out_bias[:]).then_inc(vrT_ready, 1)

            def values(n, u):
                act.wait_ge(v_made, UNITS * n + u + 1)
                for p in range(PARS):
                    rows = slice(HALF * p, HALF * (p + 1))
                    nc.scalar.copy(v_bd[rows, u, :, :, p, 0:DIM].rearrange("k s h d -> k (s h) d"),
                                   v_ps[u][rows].rearrange("k (b d) -> k b d", d=DIM)).then_inc(v_ready, 1)

            def exponentials(n, u):
                act.wait_ge(shifted, UNITS * n + u + 1)
                nc.scalar.activation(pT[:, u].rearrange("k s c -> k (s c)"), s_ps[u], ACT.Exp,
                                     scale=SCALE).then_inc(p_ready, 1)

            round_x(0, 0)
            round_x(1, 1)
            act.wait_ge(masks_made, ALL_MASKS)
            act.wait_ge(cleared, 2)
            act.wait_ge(biases_loaded, 16 * 4)
            act.wait_ge(biases_added, 1)
            queries(0, 0)
            keys(0, 0)

            def group(n, place):
                values_T(n, place)
                residual_T(n, place)
                if exists(n + 2):
                    round_x(n + 2, place + 2)
                if not before(n, 1):
                    values(n - 1, 1)
                    exponentials(n - 1, 1)
                if exists(n + 1):
                    keys(n + 1, place + 1)
                    queries(n + 1, place + 1)
                exponentials(n, 0)
                values(n, 0)

            every_group(act, group)
            values(STEPS - 1, 1)
            exponentials(STEPS - 1, 1)

        @block.vector
        def _(dve):
            nc.vector.memset(o_bank[1][:], 1.0).then_inc(banks_set, 1)
            for tile in (qT_bd, vT):
                nc.vector.memset(tile[:], 0.0).then_inc(cleared, 1)
            dve.wait_ge(w_rounded, 1)
            nc.vector.tensor_tensor(w_low[:].rearrange("e w c -> e (w c)"), o_bank[0][:],
                                    w_high[:].rearrange("e w c -> e (w c)").bitcast(F32),
                                    ALU.subtract).then_inc(w_split, 1)
            dve.wait_ge(w_split, 1)
            nc.vector.memset(o_bank[0][:], 1.0).then_inc(banks_set, 1)

            def turn(n, place, u):
                dve.wait_ge(x_turned, UNITS * n + u + 1)
                if not before(n, 3):
                    dve.wait_ge(scores_made, UNITS * (n - 3) + u + 1)
                if not before(n, 2):
                    dve.wait_ge(x_lowered, SLOTS * (n - 1))
                nc.vector.tensor_copy(xT[:, place % 2, u],
                                      t_ps[u].rearrange("e (p f) -> e p f", p=PARS)[:, :, 0:FIELDS])\
                    .then_inc(xT_ready, 1)

            def queries(n, place):
                dve.wait_ge(q_made, n + 1)
                for h in range(ACT_HEADS, HEADS):
                    rows = slice(DIM * h, DIM * (h + 1))
                    nc.vector.tensor_scalar(qT_bd[rows, place % 2, :, :, :, h, :].rearrange("d s u p f -> d (s u p) f"),
                                            q_ps[rows].rearrange("d (b f) -> d b f", f=FIELDS),
                                            biases[rows, 0:1], None, ALU.add).then_inc(q_dve, 1)

            def repeat_keys(n, place):
                dve.wait_ge(k_ready, n + 1)
                k_cols = kT[:, place % 2].rearrange("d s u p f -> d (s u p) f")
                nc.vector.tensor_copy(k_cols[:, :, FIELDS:HALF],
                                      k_cols[:, :, 0:HALF - FIELDS]).then_inc(k_again, 1)

            def max_of_quadrant(n, u):
                dve.wait_ge(scores_made, UNITS * n + u + 1)
                nc.vector.tensor_reduce(m_part[:, u], s_ps[u].rearrange("k (b c) -> k b c", c=QUAD),
                                        AX.X, ALU.max, apply_transpose=True).then_inc(m_parted, 1)

            def swap_quadrants(n, u):
                dve.wait_ge(m_parted, UNITS * n + u + 1)
                for g in range(0, P // QUAD, 2):
                    to, of = QUAD * g, QUAD * (g + 1)
                    nc.vector.tensor_copy(m_swap[to:to + QUAD, u], m_part[of:of + QUAD, u]).then_inc(m_swapped, 1)

            def max_of_keys(n, u):
                dve.wait_ge(m_swapped, 2 * (UNITS * n + u + 1))
                if not before(n, 1):
                    dve.wait_ge(diag_ready, UNITS * (n - 1) + u + 1)
                nc.vector.tensor_tensor(m_split[:, u], m_part[:, u], m_swap[:, u], ALU.max).then_inc(m_done, 1)
                nc.vector.tensor_tensor(m_high[:, u], m_part[:, u], m_swap[:, u], ALU.max).then_inc(m_done, 1)

            def max_in_parts(n, u):
                dve.wait_ge(m_done, 2 * (UNITS * n + u + 1))
                for g in range(0, P // QUAD, 2):
                    of, to = slice(QUAD * g, QUAD * (g + 1)), slice(QUAD * (g + 1), QUAD * (g + 2))
                    nc.vector.tensor_tensor(m_split[to, u], m_split[of, u], m_high[of, u],
                                            ALU.subtract).then_inc(m_ready, 1)

            def reciprocals(n, u):
                dve.wait_ge(o_made, UNITS * n + u + 1)
                o = o_ps[u].rearrange("r (b v) -> r b v", v=VW)
                nc.vector.reciprocal(r_sum[:, u], o[:, :, DIM]).then_inc(r_ready, 1)

            def normalise(n, u):
                dve.wait_ge(r_ready, UNITS * n + u + 1)
                nc.vector.tensor_tensor(y_att[:, u].rearrange("r p h d -> r h p d"),
                                        o_ps[u].rearrange("r (h p v) -> r h p v", p=PARS, v=VW)[:, :, :, 0:DIM],
                                        r_sum[:, u].rearrange("r (h p) -> r h p", p=PARS).unsqueeze(3)
                                        .to_broadcast([P, HEADS, PARS, DIM]),
                                        ALU.mult).then_inc(att_ready, 1)

            def add_residual(n, u):
                dve.wait_ge(att_ready, UNITS * n + u + 1)
                if not before(n, 1):
                    dve.wait_ge(y_ready, UNITS * (n - 1) + u + 1)
                nc.vector.tensor_tensor(y_sum[:, u], r_ps[u], y_att[:, u].rearrange("r p h d -> r (p h d)"),
                                        ALU.add).then_inc(sum_ready, 1)

            for n in range(3):
                for u in range(UNITS):
                    turn(n, n, u)
            dve.wait_ge(masks_made, ALL_MASKS)
            dve.wait_ge(cleared, 2)
            dve.wait_ge(biases_loaded, 16 * 4)
            nc.vector.tensor_tensor(out_bias[:], biases[:, 2:3], biases[:, 3:4], ALU.add).then_inc(biases_added, 1)
            queries(0, 0)
            repeat_keys(0, 0)

            def group(n, place):
                max_of_quadrant(n, 0)
                if exists(n + 3):
                    turn(n + 3, place + 3, 0)
                swap_quadrants(n, 0)
                max_of_keys(n, 0)
                max_in_parts(n, 0)
                if exists(n + 1):
                    queries(n + 1, place + 1)
                if not before(n, 1):
                    reciprocals(n - 1, 0)
                    normalise(n - 1, 0)
                    add_residual(n - 1, 0)
                max_of_quadrant(n, 1)
                if not before(n, 1):
                    reciprocals(n - 1, 1)
                swap_quadrants(n, 1)
                if exists(n + 1):
                    repeat_keys(n + 1, place + 1)
                max_of_keys(n, 1)
                if not before(n, 1):
                    normalise(n - 1, 1)
                max_in_parts(n, 1)
                if not before(n, 1):
                    add_residual(n - 1, 1)
                if exists(n + 3):
                    turn(n + 3, place + 3, 1)

            every_group(dve, group)
            for u in range(UNITS):
                reciprocals(STEPS - 1, u)
                normalise(STEPS - 1, u)
                add_residual(STEPS - 1, u)

        @block.tensor
        def _(pe):
            pe.wait_ge(w_loaded, 16 * 4)
            pe.wait_ge(masks_made, WEIGHT_MASKS)
            for w in range(4):
                last_one = nc.tensor.transpose(o_bank[0][:, w * P:(w + 1) * P],
                                               w_in[:, w].rearrange("o s e -> o (s e)"), ident[:])
            last_one.then_inc(w_turned, 1)

            def turn(n, place, u):
                rows = HALF + FIELDS
                nc.tensor.transpose(t_ps[u][:, 0:rows], x_rows[0:rows, place % 2, u].rearrange("r s e -> r (s e)"),
                                    ident[0:rows, 0:rows]).then_inc(x_turned, 1)

            def project(ps, w, x_cols, made):
                nc.tensor.matmul(ps, w_high[:, w], x_cols, start=True, stop=False)
                nc.tensor.matmul(ps, w_low[:, w], x_cols, start=False, stop=True).then_inc(made, 1)

            def queries_and_keys(n, place):
                pe.wait_ge(x_lowered, SLOTS * (n + 1))
                x_cols = x_split[:, place % SPLITS].rearrange("e s u p f -> e (s u p f)")
                project(k_ps, 1, x_cols, k_made)
                project(q_ps, 0, x_cols, q_made)

            def values_and_residual(n, place):
                pe.wait_ge(k_ready, n + 1)
                pe.wait_ge(q_act, ACT_HEADS * (n + 1))
                pe.wait_ge(q_dve, (HEADS - ACT_HEADS) * (n + 1))
                x_cols = x_split[:, place % SPLITS]
                project(vT_ps, 2, x_cols.rearrange("e s u p f -> e u s (p f)"), vT_made)
                project(rT_ps, 3, x_cols.rearrange("e s u p f -> e (u p) s f"), rT_made)

            def scores(n, place, u):
                for s in range(SLOTS):
                    for p in range(PARS):
                        mm = nc.tensor.matmul(s_ps[u][HALF * p:HALF * (p + 1), s * HQ:(s + 1) * HQ],
                                              kT[:, place % 2, s, u, p],
                                              qT_bd[:, place % 2, s, u, p].rearrange("d h f -> d (h f)"),
                                              start=(s == 0), stop=False, skip_group_check=True)
                mm.then_inc(scores_made, 1)

            def turn_back(n, place, u):
                if not before(n, 1):
                    pe.wait_ge(sum_ready, UNITS * (n - 1) + u + 1)
                for s in range(SLOTS):
                    nc.tensor.transpose(v_ps[u][:, s * OUT:(s + 1) * OUT],
                                        vT[:, place % 2, u, s].rearrange("d p f -> d (p f)"), ident[:])
                for p in range(PARS):
                    mm = nc.tensor.transpose(r_ps[u][:, p * OUT:(p + 1) * OUT],
                                             rT[:, place % 2, u, p].rearrange("d s f -> d (s f)"), ident[:])
                mm.then_inc(v_made, 1)

            def shift(n, u):
                pe.wait_ge(diag_ready, UNITS * n + u + 1)
                nc.tensor.matmul(s_ps[u], pick_par[:], m_diag[:, u].rearrange("k b c -> k (b c)"),
                                 start=False, stop=True, skip_group_check=True).then_inc(shifted, 1)

            def attend(n, u):
                pe.wait_ge(p_ready, UNITS * n + u + 1)
                pe.wait_ge(v_ready, 2 * (UNITS * n + u + 1))
                for h in range(HEADS):
                    for s in range(SLOTS):
                        mm = nc.tensor.matmul(o_ps[u][HALF * s:HALF * s + FIELDS, h * PARS * VW:(h + 1) * PARS * VW],
                                              pT[:, u, s, h * FIELDS:(h + 1) * FIELDS],
                                              v_bd[:, u, s, h].rearrange("k p v -> k (p v)"),
                                              start=True, stop=True)
                mm.then_inc(o_made, 1)

            for n in range(3):
                pe.wait_ge(x_loaded[n % 2], 32 * of_parity(n, n))
                if n > 0:
                    pe.wait_ge(xT_ready, UNITS * n)
                for u in range(UNITS):
                    turn(n, n, u)
            pe.wait_ge(w_split, 1)
            pe.wait_ge(masks_made, ALL_MASKS)
            queries_and_keys(0, 0)
            pe.wait_ge(banks_set, 2)
            pe.wait_ge(xT_ready, 3 * UNITS)

            def turn_and_scores(n, place, u):
                if not before(n, 1):
                    pe.wait_ge(p_ready, UNITS * (n - 1) + u + 1)
                if exists(n + 3):
                    if u == 0:
                        pe.wait_ge(x_loaded[(place + 3) % 2], 32 * of_parity(n + 3, place + 3))
                    turn(n + 3, place + 3, u)
                scores(n, place, u)

            def group(n, place):
                values_and_residual(n, place)
                pe.wait_ge(k_again, n + 1)
                turn_and_scores(n, place, 0)
                if not before(n, 1):
                    turn_back(n - 1, place + 1, 1)
                    if exists(n + 2):
                        pe.wait_ge(xT_ready, UNITS * (n + 3))
                    shift(n - 1, 1)
                pe.wait_ge(vrT_ready, 2 * (n + 1))
                if exists(n + 1):
                    queries_and_keys(n + 1, place + 1)
                if not before(n, 1):
                    attend(n - 1, 0)
                turn_and_scores(n, place, 1)
                if not before(n, 1):
                    attend(n - 1, 1)
                shift(n, 0)
                turn_back(n, place, 0)

            every_group(pe, group)
            turn_back(STEPS - 1, STEPS - 1, 1)
            shift(STEPS - 1, 1)
            for u in range(UNITS):
                attend(STEPS - 1, u)


_INS = ["r_x", "L0_rec_Wq", "L0_rec_bq", "L0_rec_Wk", "L0_rec_bk", "L0_rec_Wv", "L0_rec_bv", "L0_rec_Wr", "L0_rec_br"]


def kernel(**inputs):
    import numpy as np
    import concourse.bacc as bacc
    from concourse import mybir as _mybir
    from concourse.bass_utils import run_bass_kernel_spmd

    nc = bacc.Bacc("TRN2", target_bir_lowering=False, num_devices=1)
    arrays, args = {}, []
    for name in _INS:
        a = np.ascontiguousarray(inputs[name])
        arrays[name] = a
        args.append(nc.dram_tensor(name, a.shape, _mybir.dt.from_np(a.dtype), kind="ExternalInput").ap())
    batch, fields, _ = inputs["r_x"].shape
    shape = (batch, fields, inputs["L0_rec_Wq"].shape[0])
    args.append(nc.dram_tensor("y", shape, _mybir.dt.float32, kind="ExternalOutput").ap())
    attention_kernel(nc, *args)
    r = run_bass_kernel_spmd(nc, [arrays], core_ids=[0])
    return r.results[0]["y"]
```
